# Optimizing a Trainium2 kernel written in Bass

```python
import numpy as np
import jax
import jax.numpy as jnp

def _softmax(x, axis=-1):
    return jax.nn.softmax(x, axis=axis)

def _gelu(x):
    return jax.nn.gelu(x, approximate=True)

def _silu(x):
    return jax.nn.silu(x)

def _sigmoid(x):
    return jax.nn.sigmoid(x)

def _layernorm(x, axis=-1, eps=1e-05):
    m = jnp.mean(x, axis=axis, keepdims=True)
    v = jnp.var(x, axis=axis, keepdims=True)
    return (x - m) / jnp.sqrt(v + eps)

def _scatter_add(tgt, idx, src, axis=0):
    return tgt.at[idx].add(src)

def _segment_sum(src, seg, n):
    return jax.ops.segment_sum(src, seg, n)
kernel_name = 'mk_adaln_ffn_d1_seqx_r8_59cd53'

def setup_inputs(seed: int=0):
    np.random.seed(seed)
    _w = jnp.asarray

    def _rec_inputs():
        import jax
        import jax.numpy as jnp
        _rk = jax.random.key(seed)
        x = -0.000125 + 0.9999 * jax.random.normal(jax.random.fold_in(_rk, 1), (8, 128, 512), jnp.float32)
        _lenS = 128 - jax.random.randint(jax.random.fold_in(_rk, 7), (8,), 0, max(1, 128 // 4) + 1, jnp.int32)
        _lenS2 = 128 - jax.random.randint(jax.random.fold_in(_rk, 8), (8,), 0, max(1, 128 // 4) + 1, jnp.int32)
        itok_B_0_23 = jax.random.randint(jax.random.fold_in(_rk, 11), (8,), 0, 24, jnp.int32)
        return (x, itok_B_0_23)
    x, itok_B_0_23 = _rec_inputs()

    def _L0_cond_setup():
        import jax, jax.numpy as jnp
        import numpy as np
        R = 16
        ALPHA = 32
        SCALING = ALPHA / R
        SLOTS = 32
        IN_F = 512
        OUT_F = 512
        B, T = (8, 128)
        key = jax.random.key(seed)
        k1, k2, k3, k4, k5, k6 = jax.random.split(key, 6)
        x = jax.random.normal(k1, (B, T, IN_F), dtype=jnp.float32)
        adapter_mapping = jax.random.randint(k2, (B,), 0, SLOTS, dtype=jnp.int32)
        W = jax.random.normal(k3, (OUT_F, IN_F), dtype=jnp.float32) * 0.02
        b = jax.random.normal(k4, (OUT_F,), dtype=jnp.float32) * 0.02
        lora_As = jax.random.normal(k5, (SLOTS, IN_F, R), dtype=jnp.float32) * 0.02
        lora_Bs = jax.random.normal(k6, (SLOTS, R, OUT_F), dtype=jnp.float32) * 0.02
        return {'x': x, 'adapter_mapping': adapter_mapping, 'W': W, 'b': b, 'lora_As': lora_As, 'lora_Bs': lora_Bs}
    _L0_cond_all = _L0_cond_setup()
    _L0_cond_in = {k: v for k, v in _L0_cond_all.items() if k in ('W', 'b', 'lora_As', 'lora_Bs')}
    del _L0_cond_all

    def _L0_ffn_setup():
        import jax, jax.numpy as jnp
        import numpy as np
        NUM_EXPERTS = 8
        TOP_K = 2
        RANK = 16
        LORA_ALPHA = 32
        SCALING = LORA_ALPHA / RANK
        key = jax.random.key(seed)
        ks = jax.random.split(key, 6)
        B, S, D_IN, D_OUT = (4, 256, 512, 512)
        x = jax.random.normal(ks[0], (B, S, D_IN), dtype=jnp.float32)
        W_base = jax.random.normal(ks[1], (D_OUT, D_IN), dtype=jnp.float32) * 0.02
        b_base = jax.random.normal(ks[2], (D_OUT,), dtype=jnp.float32) * 0.02
        W_router = jax.random.normal(ks[3], (NUM_EXPERTS, D_IN), dtype=jnp.float32) * 0.02
        A = jax.random.normal(ks[4], (NUM_EXPERTS, RANK, D_IN), dtype=jnp.float32) * 0.02
        Bm = jax.random.normal(ks[5], (D_OUT, RANK), dtype=jnp.float32) * 0.02
        Bm = jnp.broadcast_to(Bm, (NUM_EXPERTS, D_OUT, RANK)) * jnp.arange(1, NUM_EXPERTS + 1, dtype=jnp.float32)[:, None, None] * 0.2
        return {'x': x, 'W_base': W_base, 'b_base': b_base, 'W_router': W_router, 'A': A, 'B': Bm}
    _L0_ffn_all = _L0_ffn_setup()
    _L0_ffn_in = {k: v for k, v in _L0_ffn_all.items() if k in ('W_base', 'b_base', 'W_router', 'A', 'B')}
    del _L0_ffn_all
    return {'x': x, 'itok_B_0_23': itok_B_0_23, 'L0_cond_W': _L0_cond_in['W'], 'L0_cond_b': _L0_cond_in['b'], 'L0_cond_lora_As': _L0_cond_in['lora_As'], 'L0_cond_lora_Bs': _L0_cond_in['lora_Bs'], 'L0_ffn_W_base': _L0_ffn_in['W_base'], 'L0_ffn_b_base': _L0_ffn_in['b_base'], 'L0_ffn_W_router': _L0_ffn_in['W_router'], 'L0_ffn_A': _L0_ffn_in['A'], 'L0_ffn_B': _L0_ffn_in['B']}

def reference(x, itok_B_0_23, L0_cond_W, L0_cond_b, L0_cond_lora_As, L0_cond_lora_Bs, L0_ffn_W_base, L0_ffn_b_base, L0_ffn_W_router, L0_ffn_A, L0_ffn_B):
    import jax
    import jax.numpy as jnp

    def _L0_cond_ref(x, adapter_mapping, W, b, lora_As, lora_Bs):
        import jax, jax.numpy as jnp
        import numpy as np
        R = 16
        ALPHA = 32
        SCALING = ALPHA / R
        SLOTS = 32
        IN_F = 512
        OUT_F = 512
        B, T = (8, 128)
        base_out = jnp.einsum('bti,oi->bto', x, W) + b
        A = lora_As[adapter_mapping]
        Bm = lora_Bs[adapter_mapping]
        lora_h = jnp.einsum('bti,bir->btr', x, A)
        lora_out = jnp.einsum('btr,bro->bto', lora_h, Bm)
        return base_out + lora_out * SCALING

    def _L0_ffn_ref(x, W_base, b_base, W_router, A, B):
        import jax, jax.numpy as jnp
        import numpy as np
        NUM_EXPERTS = 8
        TOP_K = 2
        RANK = 16
        LORA_ALPHA = 32
        SCALING = LORA_ALPHA / RANK
        bs, seq, d_in = x.shape
        T = bs * seq
        xf = x.reshape(T, d_in)
        base = xf @ W_base.T + b_base
        logits = xf @ W_router.T
        rw, sel = jax.lax.top_k(logits, TOP_K)
        rw = jax.nn.softmax(rw, axis=-1)
        onehot = jax.nn.one_hot(sel, NUM_EXPERTS, dtype=rw.dtype)
        w = jnp.einsum('tk,tke->te', rw, onehot)
        h = jnp.einsum('td,erd->ter', xf, A)
        lora = jnp.einsum('ter,te,eor->to', h, w, B) * SCALING
        return (base + lora).reshape(bs, seq, -1)
    x = x + _L0_ffn_ref(_L0_cond_ref(x, itok_B_0_23, L0_cond_W, L0_cond_b, L0_cond_lora_As, L0_cond_lora_Bs), L0_ffn_W_base, L0_ffn_b_base, L0_ffn_W_router, L0_ffn_A, L0_ffn_B)
    return x

_drawn_inputs = setup_inputs


def setup_inputs(seed=0):
    import zlib

    import numpy as np

    out = dict(_drawn_inputs(seed))
    spreads = {}
    factors = {'L0_cond_b': 5.398, 'L0_ffn_b_base': 2.906, 'L0_ffn_W_router': 2.826, 'L0_ffn_A': 7.18}
    for name, (base, spread) in spreads.items():
        noise = np.random.default_rng([zlib.crc32(name.encode()), seed]).standard_normal(out[name].shape)
        drawn = base * np.exp(spread * noise) if base else spread * noise
        out[name] = jnp.asarray(drawn.astype(out[name].dtype))
    for name, factor in factors.items():
        out[name] = (out[name] * factor).astype(out[name].dtype)
    return out
```

```python
from contextlib import ExitStack

import concourse.bass as bass
from concourse import mybir

F32 = mybir.dt.float32
F32R = mybir.dt.float32r
BF16 = mybir.dt.bfloat16
I32 = mybir.dt.int32
U32 = mybir.dt.uint32
ALU = mybir.AluOpType
ACT = mybir.ActivationFunctionType

P = 128
D = 512
KB = D // P
NB = 8
R = 16
NE = 8
SLOTS = 32
SCALING = 2.0
WC = D + NE + NE * R
WH = WC // 2
TC = NE + NE * R
TA = TC + R
PAIRS = NB // 2
HALVES = 2
HT = NB * P // HALVES
OB = D // P
CH = D + WC
HSTEP = P + R
LROW, HROW, CROW = 2 * R, 4 * R, 6 * R
GK = CROW + 2


def build(nc, x, w, tbl, idx, bias, bbase, bt, out):
    with ExitStack() as ctx:
        def sb(name, shape, dt=F32):
            return ctx.enter_context(nc.sbuf_tensor(name, shape, dt))

        def sem(name):
            return ctx.enter_context(nc.semaphore(name))

        wt = sb("wt", [P, KB, CH])
        xt = sb("xt", [P, HALVES, KB, HT])
        ab = sb("ab", [P, NB, 2, KB, R])
        btt = sb("btt", [P, D])
        bcol = sb("bcol", [P, KB])
        idx_sb = sb("idx_sb", [1, NB], I32)
        wt_hi = sb("wt_hi", [P, KB, CH], F32R)
        wt_lo = sb("wt_lo", [P, KB, CH], F32R)
        x_hi = sb("x_hi", [P, HALVES, KB, HT], F32R)
        x_lo = sb("x_lo", [P, HALVES, KB, HT], F32R)
        as_hl = sb("as_hl", [P, NB, KB, 2, R], F32R)
        bs_hi = sb("bs_hi", [P, KB, NB, R], F32R)
        bs_lo = sb("bs_lo", [P, KB, NB, R], F32R)
        bt_hi = sb("bt_hi", [P, D], F32R)
        bt_lo = sb("bt_lo", [P, D], F32R)
        m_hi = sb("m_hi", [P, KB, D], F32R)
        m_lo = sb("m_lo", [P, KB, D], F32R)
        rt = sb("rt", [P, 2, KB, 2, TA], F32R)
        g_hl = sb("g_hl", [P, 2, WC], F32R)
        g_st = sb("g_st", [P, PAIRS, WC], F32R)
        bsum = sb("bsum", [P, WC])
        bsum_hl = sb("bsum_hl", [P, 2, WC], F32R)
        part = sb("part", [P, PAIRS, 2, TA])
        h_sum = sb("h_sum", [P, PAIRS, 2, R])
        h_stack = sb("h_stack", [P, PAIRS, 2 * HSTEP])
        h_t = sb("h_t", [P, PAIRS, 2, P], F32R)
        full = sb("full", [P, PAIRS, 2, TC])
        top = sb("top", [P, PAIRS, 2, 8])
        top_at = sb("top_at", [P, PAIRS, 2, 8], U32)
        onehot = sb("onehot", [P, PAIRS, 2, 2, NE])
        diff = sb("diff", [P, PAIRS, 2])
        expd = sb("expd", [P, PAIRS, 2])
        den = sb("den", [P, PAIRS, 2])
        wk = sb("wk", [P, PAIRS, 2, 2])
        whot = sb("whot", [P, PAIRS, 2, 2, NE])
        we = sb("we", [P, PAIRS, 2, NE])
        hw = sb("hw", [P, PAIRS, 2, P])
        hw_hi = sb("hw_hi", [P, HALVES, HT], F32R)
        hw_lo = sb("hw_lo", [P, HALVES, HT], F32R)
        ident = sb("ident", [P, P])
        ones = sb("ones", [P, P])
        ones_r = sb("ones_r", [P, P], F32R)
        iota = sb("iota", [P, NE])
        idle = sb("idle", [P, HT], BF16)

        ps = ctx.enter_context(nc.psum_tensor("ps", [P, 8, 512], F32))
        G_BANK, C_BANK, T_BANK = 0, 2, 4

        def t_banks(p):
            b = T_BANK + 2 * (p % 2)
            return ps[:, b:b + 2, :]

        w_in = [sem(f"w_in{k}") for k in range(KB + 1)]
        idx_in = sem("idx_in")
        ab_in = sem("ab_in")
        x_in = [sem(f"x_in{h}") for h in range(HALVES)]
        bt_in = sem("bt_in")
        bias_in = sem("bias_in")
        bbase_in = sem("bbase_in")
        bsum_zero = sem("bsum_zero")
        idle_zero = sem("idle_zero")
        const = sem("const")
        id_zero = sem("id_zero")
        ones_rounded = sem("ones_rounded")
        w0_hi_done = sem("w0_hi_done")
        w_hi_done = sem("w_hi_done")
        wc_hi_done = sem("wc_hi_done")
        w_lo_done = sem("w_lo_done")
        wc_lo_done = sem("wc_lo_done")
        ab_hi_done = sem("ab_hi_done")
        ab_lo_done = sem("ab_lo_done")
        bt_hi_done = sem("bt_hi_done")
        bt_lo_done = sem("bt_lo_done")
        x_hi_done = sem("x_hi_done")
        x_lo_pool = sem("x_lo_pool")
        x_lo_dve = sem("x_lo_dve")
        m_done = sem("m_done")
        m_hi_done = sem("m_hi_done")
        m_lo_done = sem("m_lo_done")
        bsum_done = sem("bsum_done")
        bsum_hi_done = sem("bsum_hi_done")
        bsum_lo_done = sem("bsum_lo_done")
        g_done = sem("g_done")
        g_hi_done = sem("g_hi_done")
        g_lo_done = sem("g_lo_done")
        c_done = sem("c_done")
        c_hi_done = sem("c_hi_done")
        c_lo_done = sem("c_lo_done")
        gst_in = [sem(f"gst_in{p}") for p in range(PAIRS)]
        cst_in = sem("cst_in")
        as_put = sem("as_put")
        t_done = sem("t_done")
        part_done = sem("part_done")
        stack_done = sem("stack_done")
        ht_ps = sem("ht_ps")
        ht_done = sem("ht_done")
        slot_done = sem("slot_done")
        diff_done = sem("diff_done")
        exp_done = sem("exp_done")
        hw_done = sem("hw_done")
        hwt_ps = sem("hwt_ps")
        hw_hi_done = sem("hw_hi_done")
        hw_lo_done = sem("hw_lo_done")
        dve_step = sem("dve_step")
        f_done = sem("f_done")
        out_ready = sem("out_ready")
        out_written = sem("out_written")

        block = ctx.enter_context(nc.Block())

        @block.sync
        def _(sp):
            sp.dma_start(wt[:, 0, 0:D + WH], w[:, 0, 0:D + WH]).then_inc(w_in[0], 16)
            sp.dma_start(wt[:, 0, D + WH:CH], w[:, 0, D + WH:CH]).then_inc(w_in[KB], 16)
            sp.dma_start(idx_sb[:], idx).then_inc(idx_in, 16)
            for k in range(1, KB):
                sp.dma_start(wt[:, k, :], w[:, k, :]).then_inc(w_in[k], 16)
            sp.wait_ge(idx_in, 16)
            for b in range(NB):
                slot = sp.value_load(idx_sb[0:1, b:b + 1], min_val=0, max_val=SLOTS - 1)
                sp.dma_start(ab[:, b].rearrange("p c k r -> p (c k r)"),
                             tbl[bass.ds(slot, 1)].rearrange("s p n -> (s p) n")).then_inc(ab_in, 16)
            sp.dma_start(btt[:], bt).then_inc(bt_in, 16)
            for p in range(PAIRS):
                rows = slice(2 * R * p, 2 * R * (p + 1))
                if p == 0:
                    sp.wait_ge(g_hi_done, 2)
                sp.dma_start(g_st[0:LROW, p, :].bitcast(F32),
                             g_hl[rows, 0, :].bitcast(F32)).then_inc(gst_in[p], 16)
                sp.dma_start(g_st[HROW:CROW, p, :].bitcast(F32),
                             g_hl[rows, 0, :].bitcast(F32)).then_inc(gst_in[p], 16)
                if p == 0:
                    sp.wait_ge(g_lo_done, 2)
                sp.dma_start(g_st[LROW:HROW, p, :].bitcast(F32),
                             g_hl[rows, 1, :].bitcast(F32)).then_inc(gst_in[p], 16)
                if p == 0:
                    sp.wait_ge(c_hi_done, 2)
                    sp.wait_ge(c_lo_done, 2)
                    for i in range(2):
                        sp.dma_start(g_st[CROW + i:CROW + i + 1, :, :].bitcast(F32),
                                     bsum_hl[0:1, i:i + 1, :].bitcast(F32).to_broadcast([1, PAIRS, WC])
                                     ).then_inc(cst_in, 16)
            for j in range(NB):
                sp.wait_ge(out_ready, j + 1)
                sp.dma_start(out[j], xt[:, j // OB, j % OB, :]).then_inc(out_written, 16)
            sp.wait_ge(out_written, 16 * NB)

        @block.gpsimd
        def _(pool):
            nc.gpsimd.memset(idle[:], 0.0).then_inc(idle_zero, 1)
            nc.gpsimd.memset(bsum[:], 0.0).then_inc(bsum_zero, 1)
            nc.gpsimd.memset(ident[:], 0.0).then_inc(id_zero, 1)
            nc.gpsimd.memset(ones[:], 1.0).then_inc(const, 1)
            nc.gpsimd.memset(h_stack[:], 0.0).then_inc(id_zero, 1)
            pool.wait_ge(id_zero, 2)
            nc.gpsimd.affine_select(out=ident[:], in_=ident[:], compare_op=ALU.not_equal, fill=1.0, base=0,
                                    pattern=[[-1, P]], channel_multiplier=1).then_inc(const, 1)
            for t in range(2):
                nc.gpsimd.memset(h_stack[:, :, t * P + CROW:t * P + GK], 1.0 / SCALING).then_inc(const, 1)
            nc.gpsimd.iota(iota[:], pattern=[[1, NE]], base=0, channel_multiplier=0,
                           allow_small_or_imprecise_dtypes=True).then_inc(const, 1)
            for k in range(KB):
                pool.wait_ge(x_hi_done, k + 1)
                nc.gpsimd.tensor_tensor(x_lo[:, 0, k, :], xt[:, 0, k, :], x_hi[:, 0, k, :].bitcast(F32),
                                        ALU.subtract).then_inc(x_lo_pool, 1)
            pool.wait_ge(ab_hi_done, 2)
            pool.wait_ge(ab_lo_done, 2)
            for b in range(NB):
                if b >= 2:
                    pool.wait_ge(t_done, b - 1)
                nc.gpsimd.tensor_copy(rt[:, b % 2, :, :, TC:TA], as_hl[:, b].bitcast(F32)).then_inc(as_put, 1)

        @block.scalar
        def _(act):
            def hi(dst, src):
                return nc.scalar.activation(dst, src, ACT.Copy)

            act.dma_start(bcol[:], bias).then_inc(bias_in, 16)
            act.wait_ge(bsum_zero, 1)
            act.dma_start(bsum[0:1, 0:D], bbase).then_inc(bbase_in, 16)
            act.wait_ge(w_in[0], 16)
            hi(wt_hi[:, 0, D:D + WH], wt[:, 0, D:D + WH]).then_inc(wc_hi_done, 1)
            act.wait_ge(w_in[KB], 16)
            hi(wt_hi[:, 0, D + WH:CH], wt[:, 0, D + WH:CH]).then_inc(wc_hi_done, 1)
            for h in range(HALVES):
                for k in range(0, KB, 2):
                    act.dma_start(xt[:, h, k:k + 2, :], x[:, h, k:k + 2, :]).then_inc(x_in[h], 16)
            for k in range(1, KB):
                act.wait_ge(w_in[k], 16)
                hi(wt_hi[:, k, D:CH], wt[:, k, D:CH]).then_inc(wc_hi_done, 1)
                hi(wt_hi[:, k, 0:D], wt[:, k, 0:D]).then_inc(w_hi_done, 1)
            act.wait_ge(ab_in, 16 * NB)
            hi(bs_hi[:].rearrange("p k b r -> p b k r"), ab[:, :, 1]).then_inc(ab_hi_done, 1)
            hi(as_hl[:, :, :, 0, :], ab[:, :, 0]).then_inc(ab_hi_done, 1)
            act.wait_ge(x_in[0], 32)
            for k in range(KB):
                hi(x_hi[:, 0, k, :], xt[:, 0, k, :]).then_inc(x_hi_done, 1)
            act.wait_ge(bt_in, 16)
            hi(bt_hi[:], btt[:]).then_inc(bt_hi_done, 1)
            act.wait_ge(bsum_done, KB)
            hi(bsum_hl[:, 0], bsum[:]).then_inc(bsum_hi_done, 1)
            for i in range(KB):
                act.wait_ge(m_done, i + 1)
                hi(m_hi[:, i, 0:WH], ps[:, 2 * i, 0:WH]).then_inc(m_hi_done, 1)
                hi(m_hi[:, i, WH:D], ps[:, 2 * i + 1, 0:D - WH]).then_inc(m_hi_done, 1)
                hi(rt[:, :, i, 0, 0:TC],
                   ps[:, 2 * i + 1:2 * i + 2, D - WH:WH].to_broadcast([P, 2, TC])).then_inc(m_hi_done, 1)
            act.wait_ge(g_done, 1)
            for s in range(2):
                hi(g_hl[:, 0, s * WH:(s + 1) * WH], ps[:, G_BANK + s, 0:WH]).then_inc(g_hi_done, 1)
            act.wait_ge(c_done, 1)
            for s in range(2):
                hi(bsum_hl[0:1, 0, s * WH:(s + 1) * WH], ps[0:1, C_BANK + s, 0:WH]).then_inc(c_hi_done, 1)
            act.wait_ge(x_in[1], 32)
            for k in range(KB):
                hi(x_hi[:, 1, k, :], xt[:, 1, k, :]).then_inc(x_hi_done, 1)

            def take_part(p):
                act.wait_ge(t_done, 2 * (p + 1))
                nc.scalar.activation(part[:, p], t_banks(p)[:, :, TA:2 * TA], ACT.Copy).then_inc(part_done, 1)

            def stack_t(p):
                act.wait_ge(ht_ps, p + 1)
                nc.scalar.activation(h_t[0:GK, p], t_banks(p)[0:GK, :, 2 * TA:2 * TA + P], ACT.Copy,
                                     scale=SCALING).then_inc(ht_done, 1)

            def exps(p):
                act.wait_ge(diff_done, p + 1)
                nc.scalar.activation(expd[:, p], diff[:, p], ACT.Exp).then_inc(exp_done, 1)

            def weighted_hi(p):
                act.wait_ge(hwt_ps, p + 1)
                hi(hw_hi[:, p // 2, (p % 2) * 2 * P:(p % 2 + 1) * 2 * P].rearrange("e (t n) -> e t n", t=2),
                   t_banks(p)[:, :, 2 * TA:2 * TA + P]).then_inc(hw_hi_done, 1)

            take_part(0)
            take_part(1)
            stack_t(0)
            stack_t(1)
            exps(0)
            exps(1)
            weighted_hi(0)
            weighted_hi(1)
            take_part(2)
            stack_t(2)
            exps(2)
            take_part(3)
            stack_t(3)
            exps(3)
            weighted_hi(2)
            weighted_hi(3)

        @block.vector
        def _(dve):
            steps = [0]

            def link(ins):
                steps[0] += 1
                ins.then_inc(dve_step, 1)
                dve.wait_ge(dve_step, steps[0])

            def lo(dst, src, high):
                return nc.vector.tensor_tensor(dst, src, high.bitcast(F32), ALU.subtract)

            dve.wait_ge(w_in[0], 16)
            nc.vector.tensor_copy(wt_hi[:, 0, 0:D], wt[:, 0, 0:D]).then_inc(w0_hi_done, 1)
            for k in range(KB):
                if k == 0:
                    for s in range(2):
                        dve.wait_ge(wc_hi_done, s + 1)
                        c = slice(D + s * WH, D + (s + 1) * WH)
                        lo(wt_lo[:, 0, c], wt[:, 0, c], wt_hi[:, 0, c]).then_inc(wc_lo_done, 1)
                else:
                    dve.wait_ge(wc_hi_done, k + 2)
                    lo(wt_lo[:, k, D:CH], wt[:, k, D:CH], wt_hi[:, k, D:CH]).then_inc(wc_lo_done, 1)
                if k == 0:
                    dve.wait_ge(w0_hi_done, 1)
                else:
                    dve.wait_ge(w_hi_done, k)
                lo(wt_lo[:, k, 0:D], wt[:, k, 0:D], wt_hi[:, k, 0:D]).then_inc(w_lo_done, 1)
                if k == 0:
                    dve.wait_ge(const, 1)
                    nc.vector.tensor_copy(ones_r[:], ones[:]).then_inc(ones_rounded, 1)
                    dve.wait_ge(bias_in, 16)
                    dve.wait_ge(bbase_in, 16)
                else:
                    dve.wait_ge(bsum_done, k)
                nc.vector.scalar_tensor_tensor(out=bsum[:], in0=wt[:, k, D:CH], scalar=bcol[:, k:k + 1],
                                               in1=bsum[:], op0=ALU.mult, op1=ALU.add).then_inc(bsum_done, 1)
            dve.wait_ge(ab_hi_done, 1)
            lo(bs_lo[:].rearrange("p k b r -> p b k r"), ab[:, :, 1],
               bs_hi[:].rearrange("p k b r -> p b k r")).then_inc(ab_lo_done, 1)
            dve.wait_ge(ab_hi_done, 2)
            lo(as_hl[:, :, :, 1, :], ab[:, :, 0], as_hl[:, :, :, 0, :]).then_inc(ab_lo_done, 1)
            dve.wait_ge(bsum_hi_done, 1)
            lo(bsum_hl[:, 1], bsum[:], bsum_hl[:, 0]).then_inc(bsum_lo_done, 1)
            dve.wait_ge(bt_hi_done, 1)
            lo(bt_lo[:], btt[:], bt_hi[:]).then_inc(bt_lo_done, 1)
            for i in range(KB):
                dve.wait_ge(m_hi_done, 3 * i + 1)
                lo(m_lo[:, i, 0:WH], ps[:, 2 * i, 0:WH], m_hi[:, i, 0:WH]).then_inc(m_lo_done, 1)
                dve.wait_ge(m_hi_done, 3 * i + 3)
                lo(m_lo[:, i, WH:D], ps[:, 2 * i + 1, 0:D - WH], m_hi[:, i, WH:D]).then_inc(m_lo_done, 1)
                lo(rt[:, :, i, 1, 0:TC], ps[:, 2 * i + 1:2 * i + 2, D - WH:WH].to_broadcast([P, 2, TC]),
                   rt[:, :, i, 0, 0:TC]).then_inc(m_lo_done, 1)
            for s in range(2):
                dve.wait_ge(g_hi_done, s + 1)
                c = slice(s * WH, (s + 1) * WH)
                lo(g_hl[:, 1, c], ps[:, G_BANK + s, 0:WH], g_hl[:, 0, c]).then_inc(g_lo_done, 1)
            for s in range(2):
                dve.wait_ge(c_hi_done, s + 1)
                c = slice(s * WH, (s + 1) * WH)
                lo(bsum_hl[0:1, 1, c], ps[0:1, C_BANK + s, 0:WH], bsum_hl[0:1, 0, c]).then_inc(c_lo_done, 1)
            for k in range(KB):
                dve.wait_ge(x_hi_done, KB + k + 1)
                lo(x_lo[:, 1, k, :], xt[:, 1, k, :], x_hi[:, 1, k, :]).then_inc(x_lo_dve, 1)

            def stack(p):
                hs = h_stack[:, p].rearrange("p (t c) -> p t c", t=2)
                dve.wait_ge(part_done, p + 1)
                link(nc.vector.tensor_tensor(h_sum[:, p], t_banks(p)[:, :, TC:TA], part[:, p, :, TC:TA], ALU.add))
                if p == 0:
                    dve.wait_ge(const, 5)
                for at in (0, LROW):
                    last = nc.vector.tensor_copy(hs[:, :, at:at + R].bitcast(F32R), h_sum[:, p])
                    if at == 0:
                        link(last)
                nc.vector.tensor_tensor(hs[:, :, HROW:HROW + R].bitcast(F32R), h_sum[:, p],
                                        hs[:, :, 0:R], ALU.subtract).then_inc(stack_done, 1)

            def route(p):
                dve.wait_ge(slot_done, p + 1)
                link(nc.vector.tensor_tensor(full[:, p], t_banks(p)[:, :, 0:TC], part[:, p, :, 0:TC], ALU.add))
                for t in range(2):
                    link(nc.vector.max(top[:, p, t, :], full[:, p, t, 0:NE]))
                nc.vector.tensor_tensor(diff[:, p], top[:, p, :, 1], top[:, p, :, 0],
                                        ALU.subtract).then_inc(diff_done, 1)
                for t in range(2):
                    link(nc.vector.max_index(top_at[:, p, t, :], top[:, p, t, :], full[:, p, t, 0:NE]))
                for t in range(2):
                    link(nc.vector.tensor_tensor(
                        onehot[:, p, t], iota[:, None, :].to_broadcast([P, 2, NE]),
                        top_at[:, p, t, 0:2, None].to_broadcast([P, 2, NE]), ALU.is_equal))
                dve.wait_ge(exp_done, p + 1)
                link(nc.vector.tensor_scalar(den[:, p], expd[:, p], 1.0 / SCALING, 1.0 / SCALING,
                                             ALU.mult, ALU.add))
                link(nc.vector.reciprocal(wk[:, p, :, 0], den[:, p]))
                link(nc.vector.tensor_tensor(wk[:, p, :, 1], wk[:, p, :, 0], expd[:, p], ALU.mult))
                link(nc.vector.tensor_tensor(whot[:, p], onehot[:, p],
                                             wk[:, p, :, :, None].to_broadcast([P, 2, 2, NE]), ALU.mult))
                link(nc.vector.tensor_tensor(we[:, p], whot[:, p, :, 0, :], whot[:, p, :, 1, :], ALU.add))
                nc.vector.tensor_tensor(
                    hw[:, p].rearrange("p t (e r) -> p t e r", e=NE),
                    full[:, p, :, NE:TC].rearrange("p t (e r) -> p t e r", e=NE),
                    we[:, p, :, :, None].to_broadcast([P, 2, NE, R]), ALU.mult).then_inc(hw_done, 1)

            def weighted_lo(p):
                c = slice((p % 2) * 2 * P, (p % 2 + 1) * 2 * P)
                dve.wait_ge(hw_hi_done, p + 1)
                lo(hw_lo[:, p // 2, c].rearrange("e (t n) -> e t n", t=2), t_banks(p)[:, :, 2 * TA:2 * TA + P],
                   hw_hi[:, p // 2, c].rearrange("e (t n) -> e t n", t=2)).then_inc(hw_lo_done, 1)

            def finish(j):
                h, o = divmod(j, OB)
                dve.wait_ge(f_done, j + 1)
                nc.vector.tensor_tensor(xt[:, h, o, :], ps[:, j % OB, :], xt[:, h, o, :], ALU.add).then_inc(out_ready, 1)

            stack(0)
            stack(1)
            route(0)
            route(1)
            weighted_lo(0)
            weighted_lo(1)
            stack(2)
            route(2)
            stack(3)
            finish(0)
            finish(1)
            route(3)
            finish(2)
            weighted_lo(2)
            finish(3)
            weighted_lo(3)
            for j in range(OB, NB):
                finish(j)

        @block.tensor
        def _(pe):
            mm = nc.tensor.matmul
            pe.wait_ge(idle_zero, 1)
            for _ in range(9):
                mm(ps[:, 7, :], idle[:, 0:P], idle[:], start=True, stop=True)

            def m_part(k, i, s, a, c, first=False, last=False):
                return mm(ps[:, 2 * i + s, 0:WH], a[:, k, i * P:(i + 1) * P],
                          c[:, k, D + s * WH:D + (s + 1) * WH], start=first, stop=last)

            for k in range(KB - 1):
                if k == 0:
                    pe.wait_ge(w0_hi_done, 1)
                else:
                    pe.wait_ge(w_hi_done, k)
                for s in range(2):
                    pe.wait_ge(wc_hi_done, s + 1 if k == 0 else k + 2)
                    for i in range(KB):
                        m_part(k, i, s, wt_hi, wt_hi, first=(k == 0))
                pe.wait_ge(wc_lo_done, k + 2)
                for s in range(2):
                    for i in range(KB):
                        m_part(k, i, s, wt_hi, wt_lo)
                pe.wait_ge(w_lo_done, k + 1)
                for s in range(2):
                    for i in range(KB):
                        m_part(k, i, s, wt_lo, wt_hi)
            k = KB - 1
            pe.wait_ge(w_hi_done, KB - 1)
            pe.wait_ge(wc_hi_done, KB + 1)
            pe.wait_ge(wc_lo_done, KB + 1)
            pe.wait_ge(w_lo_done, KB)
            for i in range(KB):
                for s in range(2):
                    m_part(k, i, s, wt_hi, wt_hi)
                    m_part(k, i, s, wt_hi, wt_lo)
                    last = m_part(k, i, s, wt_lo, wt_hi, last=True)
                last.then_inc(m_done, 1)
            pe.wait_ge(ab_hi_done, 1)
            pe.wait_ge(ab_lo_done, 1)
            pe.wait_ge(m_lo_done, 3)
            for s in range(2):
                for k in range(KB):
                    for n, (a, c) in enumerate(((bs_hi, wt_hi), (bs_hi, wt_lo), (bs_lo, wt_hi))):
                        last = mm(ps[:, G_BANK + s, 0:WH], a[:, k].rearrange("p b r -> p (b r)"),
                                  c[:, k, D + s * WH:D + (s + 1) * WH],
                                  start=(k == 0 and n == 0), stop=(k == KB - 1 and n == 2))
            last.then_inc(g_done, 1)
            pe.wait_ge(ones_rounded, 1)
            pe.wait_ge(bsum_hi_done, 1)
            pe.wait_ge(bsum_lo_done, 1)
            pe.wait_ge(m_lo_done, 6)
            for s in range(2):
                for i in range(2):
                    last = mm(ps[:, C_BANK + s, 0:WH], ones_r[:], bsum_hl[:, i, s * WH:(s + 1) * WH],
                              start=(i == 0), stop=(i == 1))
            last.then_inc(c_done, 1)

            def router(p):
                if p == 0:
                    pe.wait_ge(m_lo_done, 3 * KB)
                    pe.wait_ge(x_hi_done, KB)
                    pe.wait_ge(x_lo_pool, KB)
                if p >= 2:
                    pe.wait_ge(hw_lo_done, p - 1)
                    pe.wait_ge(x_hi_done, 2 * KB)
                    pe.wait_ge(x_lo_dve, KB)
                for t in range(2):
                    b = 2 * p + t
                    pe.wait_ge(as_put, b + 1)
                    h, tok = b // (NB // 2), slice((b % 4) * P, (b % 4 + 1) * P)
                    for i in range(KB):
                        op = rt[:, b % 2, i].rearrange("p l c -> p (l c)")
                        mm(t_banks(p)[:, t, 0:2 * TA], x_hi[:, h, i, tok], op, start=(i == 0), stop=False,
                           skip_group_check=True)
                        last = mm(t_banks(p)[:, t, 0:TA], x_lo[:, h, i, tok], op[:, 0:TA], start=False,
                                  stop=False, skip_group_check=True)
                    last.then_inc(t_done, 1)

            def stack_transpose(p):
                if p == 0:
                    pe.wait_ge(const, 2)
                pe.wait_ge(stack_done, p + 1)
                for t in range(2):
                    last = mm(t_banks(p)[:, t, 2 * TA:2 * TA + P], h_stack[:, p, t * P:(t + 1) * P], ident[:],
                              is_transpose=True, start=False, stop=True, skip_group_check=True)
                last.then_inc(ht_ps, 1)

            def slots(p):
                if p == 0:
                    pe.wait_ge(cst_in, 32)
                pe.wait_ge(ht_done, p + 1)
                pe.wait_ge(gst_in[p], 48)
                for t in range(2):
                    last = mm(t_banks(p)[:, t, 0:TC], h_t[0:GK, p, t, :], g_st[0:GK, p, D:WC],
                              start=False, stop=True, skip_group_check=True)
                last.then_inc(slot_done, 1)

            def weighted_transpose(p):
                pe.wait_ge(hw_done, p + 1)
                for t in range(2):
                    last = nc.tensor.transpose(t_banks(p)[:, t, 2 * TA:2 * TA + P], hw[:, p, t, :], ident[:])
                last.then_inc(hwt_ps, 1)

            def base(j, part_of):
                h, o = divmod(j, OB)
                if j == 0:
                    pe.wait_ge(g_lo_done, 2)
                if j == 2:
                    pe.wait_ge(c_lo_done, 2)
                if j >= OB and part_of == 0:
                    pe.wait_ge(out_ready, j - OB + 1)
                products = [(a, v, i) for a, v in ((m_hi, x_hi), (m_lo, x_hi), (m_hi, x_lo)) for i in range(KB)]
                for n in range(6 * part_of, 6 * part_of + 6):
                    a, v, i = products[n]
                    mm(ps[:, j % OB, :], a[:, i, o * P:(o + 1) * P], v[:, h, i, :], start=(n == 0), stop=False)

            def rest(j):
                h, o = divmod(j, OB)
                oc = slice(o * P, (o + 1) * P)
                for q in range(2):
                    p = 2 * h + q
                    mm(ps[:, j % OB, q * 2 * P:(q + 1) * 2 * P], g_st[0:GK, p, oc],
                       h_t[0:GK, p].rearrange("k t n -> k (t n)"), start=False, stop=False)
                if j == 0:
                    pe.wait_ge(bt_hi_done, 1)
                    pe.wait_ge(bt_lo_done, 1)
                pe.wait_ge(hw_lo_done, 2 * (h + 1))
                mm(ps[:, j % OB, :], bt_hi[:, oc], hw_hi[:, h, :], start=False, stop=False)
                mm(ps[:, j % OB, :], bt_lo[:, oc], hw_hi[:, h, :], start=False, stop=False)
                mm(ps[:, j % OB, :], bt_hi[:, oc], hw_lo[:, h, :], start=False, stop=True).then_inc(f_done, 1)

            router(0)
            router(1)
            stack_transpose(0)
            base(0, 0)
            slots(0)
            stack_transpose(1)
            base(0, 1)
            slots(1)
            base(1, 0)
            base(1, 1)
            weighted_transpose(0)
            base(2, 0)
            base(2, 1)
            weighted_transpose(1)
            router(2)
            base(3, 0)
            stack_transpose(2)
            base(3, 1)
            slots(2)
            router(3)
            rest(0)
            stack_transpose(3)
            rest(1)
            slots(3)
            rest(2)
            weighted_transpose(2)
            rest(3)
            base(4, 0)
            base(4, 1)
            weighted_transpose(3)
            base(5, 0)
            base(5, 1)
            rest(4)
            base(6, 0)
            base(6, 1)
            rest(5)
            base(7, 0)
            base(7, 1)
            rest(6)
            rest(7)


def kernel(**inputs):
    import numpy as np
    import concourse.bacc as bacc
    from concourse.bass_utils import run_bass_kernel_spmd

    def a(name):
        return np.asarray(inputs[name])

    def blocks(m):
        return m.reshape(m.shape[0] // P, P, m.shape[1]).transpose(1, 0, 2)

    x = a("x").reshape(HALVES, HT, KB, P).transpose(3, 0, 2, 1)
    wc = np.concatenate([a("L0_ffn_W_base"), a("L0_ffn_W_router"), a("L0_ffn_A").reshape(NE * R, D)])
    w = np.concatenate([blocks(a("L0_cond_W")), blocks(wc.T)], axis=2)
    by_slot = [m.reshape(SLOTS, KB, P, R).transpose(0, 2, 1, 3).reshape(SLOTS, P, KB * R)
               for m in (a("L0_cond_lora_As"), a("L0_cond_lora_Bs").transpose(0, 2, 1))]
    arrays = {
        "x_t": x,
        "w_chunks": w,
        "adapters": np.concatenate(by_slot, axis=2),
        "slots": a("itok_B_0_23").reshape(1, NB),
        "bias": a("L0_cond_b").reshape(KB, P).T,
        "b_base": a("L0_ffn_b_base").reshape(1, D),
        "b_t": a("L0_ffn_B").transpose(0, 2, 1).reshape(NE * R, D),
    }
    arrays = {k: np.ascontiguousarray(v) for k, v in arrays.items()}
    nc = bacc.Bacc("TRN2", target_bir_lowering=False, num_devices=1)
    args = [nc.dram_tensor(k, v.shape, mybir.dt.from_np(v.dtype), kind="ExternalInput").ap()
            for k, v in arrays.items()]
    args.append(nc.dram_tensor("out_t", (NB, P, HT), F32, kind="ExternalOutput").ap())
    build(nc, *args)
    got = run_bass_kernel_spmd(nc, [arrays], core_ids=[0]).results[0]["out_t"]
    return np.asarray(got).reshape(HALVES, OB, P, HT).transpose(0, 3, 1, 2).reshape(NB, P, D)
```

```python
from contextlib import ExitStack

import concourse.bass as bass
from concourse import mybir

F32 = mybir.dt.float32
F32R = mybir.dt.float32r
BF16 = mybir.dt.bfloat16
I32 = mybir.dt.int32
U32 = mybir.dt.uint32
ALU = mybir.AluOpType
ACT = mybir.ActivationFunctionType

P = 128
D = 512
KB = D // P
NB = 8
R = 16
NE = 8
SLOTS = 32
IDLE = 29
SCALING = 2.0
WC = D + NE + NE * R
WH = WC // 2
TC = NE + NE * R
TA = TC + R
PAIRS = NB // 2
HALVES = 2
HT = NB * P // HALVES
OB = D // P
CH = D + WC
W0_PIECES = [slice(D // 2, D + WH), slice(0, D // 2), slice(D + WH, CH)]
HSTEP = P + R
LROW, HROW, CROW = 2 * R, 4 * R, 6 * R
GK = CROW + 2
PIECES = [(j, slice(0, HT)) for j in range(NB - 1)] + [(NB - 1, slice(0, HT // 2)), (NB - 1, slice(HT // 2, HT))]


def build(nc, x, w, tbl, idx, bias, bbase, bt, out):
    with ExitStack() as ctx:
        def sb(name, shape, dt=F32):
            return ctx.enter_context(nc.sbuf_tensor(name, shape, dt))

        def sem(name):
            return ctx.enter_context(nc.semaphore(name))

        wt = sb("wt", [P, KB, CH])
        xt = sb("xt", [P, HALVES, KB, HT])
        ab = sb("ab", [P, NB, 2, KB, R])
        btt = sb("btt", [P, D])
        bcol = sb("bcol", [P, KB])
        idx_sb = sb("idx_sb", [1, NB], I32)
        wt_hi = sb("wt_hi", [P, KB, CH], F32R)
        wt_lo = sb("wt_lo", [P, KB, CH], F32R)
        x_hi = sb("x_hi", [P, HALVES, KB, HT], F32R)
        x_lo = sb("x_lo", [P, HALVES, KB, HT], F32R)
        as_hl = sb("as_hl", [P, NB, KB, 2, R], F32R)
        bs_hi = sb("bs_hi", [P, KB, NB, R], F32R)
        bs_lo = sb("bs_lo", [P, KB, NB, R], F32R)
        bt_hi = sb("bt_hi", [P, D], F32R)
        bt_lo = sb("bt_lo", [P, D], F32R)
        m_hi = sb("m_hi", [P, KB, D], F32R)
        m_lo = sb("m_lo", [P, KB, D], F32R)
        rt = sb("rt", [P, 2, KB, 2, TA], F32R)
        g_hl = sb("g_hl", [P, 2, WC], F32R)
        g_st = sb("g_st", [P, PAIRS, WC], F32R)
        bsum = sb("bsum", [P, WC])
        bsum_hl = sb("bsum_hl", [P, 2, WC], F32R)
        part = sb("part", [P, PAIRS, 2, TA])
        h_sum = sb("h_sum", [P, PAIRS, 2, R])
        h_stack = sb("h_stack", [P, PAIRS, 2 * HSTEP])
        h_t = sb("h_t", [P, PAIRS, 2, P], F32R)
        full = sb("full", [P, PAIRS, 2, TC])
        top = sb("top", [P, PAIRS, 2, 8])
        top_at = sb("top_at", [P, PAIRS, 2, 8], U32)
        onehot = sb("onehot", [P, PAIRS, 2, 2, NE])
        diff = sb("diff", [P, PAIRS, 2])
        expd = sb("expd", [P, PAIRS, 2])
        den = sb("den", [P, PAIRS, 2])
        wk = sb("wk", [P, PAIRS, 2, 2])
        whot = sb("whot", [P, PAIRS, 2, 2, NE])
        we = sb("we", [P, PAIRS, 2, NE])
        hw = sb("hw", [P, PAIRS, 2, P])
        hw_hi = sb("hw_hi", [P, HALVES, HT], F32R)
        hw_lo = sb("hw_lo", [P, HALVES, HT], F32R)
        ident = sb("ident", [P, P])
        ones = sb("ones", [P, P])
        ones_r = sb("ones_r", [P, P], F32R)
        iota = sb("iota", [P, NE])
        idle = sb("idle", [P, P], BF16)

        ps = ctx.enter_context(nc.psum_tensor("ps", [P, 8, 512], F32))
        G_BANK, C_BANK, T_BANK = 0, 2, 4

        def t_banks(p):
            b = T_BANK + 2 * (p % 2)
            return ps[:, b:b + 2, :]

        def piece_ps(n):
            tok = PIECES[n][1]
            return ps[:, n % OB if n < NB else T_BANK, 0:tok.stop - tok.start]

        w0_in = [sem(f"w0_in{n}") for n in range(len(W0_PIECES))]
        w_in = [sem(f"w_in{k}") for k in range(KB)]
        idx_in = sem("idx_in")
        ab_in = sem("ab_in")
        x_in = [sem(f"x_in{h}") for h in range(HALVES)]
        bt_in = sem("bt_in")
        bias_in = sem("bias_in")
        bbase_in = sem("bbase_in")
        bsum_zero = sem("bsum_zero")
        idle_zero = sem("idle_zero")
        const = sem("const")
        id_zero = sem("id_zero")
        ones_rounded = sem("ones_rounded")
        w0_hi_done = sem("w0_hi_done")
        w_hi_done = sem("w_hi_done")
        wc_hi_done = sem("wc_hi_done")
        w_lo_done = sem("w_lo_done")
        wc_lo_done = sem("wc_lo_done")
        ab_hi_done = sem("ab_hi_done")
        ab_lo_done = sem("ab_lo_done")
        bt_hi_done = sem("bt_hi_done")
        bt_lo_done = sem("bt_lo_done")
        x_hi_done = sem("x_hi_done")
        x_lo_done = sem("x_lo_done")
        m_done = sem("m_done")
        m_hi_done = sem("m_hi_done")
        m_lo_done = sem("m_lo_done")
        bsum_done = sem("bsum_done")
        bsum_hi_done = sem("bsum_hi_done")
        bsum_lo_done = sem("bsum_lo_done")
        g_done = sem("g_done")
        g_hi_done = sem("g_hi_done")
        g_lo_done = sem("g_lo_done")
        c_done = sem("c_done")
        c_hi_done = sem("c_hi_done")
        c_lo_done = sem("c_lo_done")
        gst_in = [sem(f"gst_in{p}") for p in range(PAIRS)]
        cst_in = sem("cst_in")
        as_put = sem("as_put")
        t_done = sem("t_done")
        part_done = sem("part_done")
        stack_done = sem("stack_done")
        ht_ps = sem("ht_ps")
        ht_done = sem("ht_done")
        slot_done = sem("slot_done")
        diff_done = sem("diff_done")
        exp_done = sem("exp_done")
        hw_done = sem("hw_done")
        hwt_ps = sem("hwt_ps")
        hw_hi_done = sem("hw_hi_done")
        hw_lo_done = sem("hw_lo_done")
        dve_step = sem("dve_step")
        f_done = sem("f_done")
        out_ready = sem("out_ready")
        out_written = sem("out_written")

        block = ctx.enter_context(nc.Block())

        @block.sync
        def _(sp):
            for n, piece in enumerate(W0_PIECES):
                sp.dma_start(wt[:, 0, piece], w[:, 0, piece]).then_inc(w0_in[n], 16)
            sp.dma_start(idx_sb[:], idx).then_inc(idx_in, 16)
            sp.dma_start(bcol[:], bias).then_inc(bias_in, 16)
            for k in range(1, KB):
                sp.dma_start(wt[:, k, :], w[:, k, :]).then_inc(w_in[k], 16)
            sp.wait_ge(bsum_zero, 1)
            sp.dma_start(bsum[0:1, 0:D], bbase).then_inc(bbase_in, 16)
            sp.wait_ge(idx_in, 16)
            for b in range(NB):
                slot = sp.value_load(idx_sb[0:1, b:b + 1], min_val=0, max_val=SLOTS - 1)
                sp.dma_start(ab[:, b].rearrange("p c k r -> p (c k r)"),
                             tbl[bass.ds(slot, 1)].rearrange("s p n -> (s p) n")).then_inc(ab_in, 16)
            sp.dma_start(btt[:], bt).then_inc(bt_in, 16)
            for k in range(0, KB, 2):
                sp.dma_start(xt[:, 1, k:k + 2, :], x[:, 1, k:k + 2, :]).then_inc(x_in[1], 16)
            for p in range(PAIRS):
                rows = slice(2 * R * p, 2 * R * (p + 1))
                if p == 0:
                    sp.wait_ge(g_hi_done, 2)
                sp.dma_start(g_st[0:LROW, p, :].bitcast(F32),
                             g_hl[rows, 0, :].bitcast(F32)).then_inc(gst_in[p], 16)
                sp.dma_start(g_st[HROW:CROW, p, :].bitcast(F32),
                             g_hl[rows, 0, :].bitcast(F32)).then_inc(gst_in[p], 16)
                if p == 0:
                    sp.wait_ge(g_lo_done, 2)
                sp.dma_start(g_st[LROW:HROW, p, :].bitcast(F32),
                             g_hl[rows, 1, :].bitcast(F32)).then_inc(gst_in[p], 16)
            for n, (j, tok) in enumerate(PIECES):
                sp.wait_ge(out_ready, n + 1)
                sp.dma_start(out[j, :, tok], xt[:, j // OB, j % OB, tok]).then_inc(out_written, 16)
            sp.wait_ge(out_written, 16 * len(PIECES))

        @block.gpsimd
        def _(pool):
            nc.gpsimd.memset(bsum[:], 0.0).then_inc(bsum_zero, 1)
            nc.gpsimd.memset(ident[:], 0.0).then_inc(id_zero, 1)
            nc.gpsimd.memset(ones[:], 1.0).then_inc(const, 1)
            nc.gpsimd.memset(h_stack[:], 0.0).then_inc(id_zero, 1)
            pool.wait_ge(id_zero, 2)
            nc.gpsimd.affine_select(out=ident[:], in_=ident[:], compare_op=ALU.not_equal, fill=1.0, base=0,
                                    pattern=[[-1, P]], channel_multiplier=1).then_inc(const, 1)
            for t in range(2):
                nc.gpsimd.memset(h_stack[:, :, t * P + CROW:t * P + GK], 1.0 / SCALING).then_inc(const, 1)
            nc.gpsimd.iota(iota[:], pattern=[[1, NE]], base=0, channel_multiplier=0,
                           allow_small_or_imprecise_dtypes=True).then_inc(const, 1)
            def x_split(h):
                for k in range(KB):
                    pool.wait_ge(x_hi_done, h * KB + k + 1)
                    nc.gpsimd.tensor_tensor(x_lo[:, h, k, :], xt[:, h, k, :], x_hi[:, h, k, :].bitcast(F32),
                                            ALU.subtract).then_inc(x_lo_done, 1)

            x_split(0)
            pool.wait_ge(ab_hi_done, 2)
            pool.wait_ge(ab_lo_done, 2)
            for b in range(NB):
                if b == NB // 2:
                    pool.wait_ge(c_hi_done, 2)
                    pool.wait_ge(c_lo_done, 2)
                    for i in range(2):
                        pool.dma_start(g_st[CROW + i:CROW + i + 1, :, :].bitcast(F32),
                                       bsum_hl[0:1, i:i + 1, :].bitcast(F32).to_broadcast([1, PAIRS, WC])
                                       ).then_inc(cst_in, 16)
                    x_split(1)
                if b >= 2:
                    pool.wait_ge(t_done, b - 1)
                nc.gpsimd.tensor_copy(rt[:, b % 2, :, :, TC:TA], as_hl[:, b].bitcast(F32)).then_inc(as_put, 1)

        @block.scalar
        def _(act):
            def hi(dst, src):
                return nc.scalar.activation(dst, src, ACT.Copy)

            act.wait_ge(w0_in[0], 16)
            hi(wt_hi[:, 0, D:D + WH], wt[:, 0, D:D + WH]).then_inc(wc_hi_done, 1)
            act.wait_ge(w0_in[2], 16)
            hi(wt_hi[:, 0, D + WH:CH], wt[:, 0, D + WH:CH]).then_inc(wc_hi_done, 1)
            for k in range(1, KB):
                act.wait_ge(w_in[k], 16)
                hi(wt_hi[:, k, D:CH], wt[:, k, D:CH]).then_inc(wc_hi_done, 1)
                hi(wt_hi[:, k, 0:D], wt[:, k, 0:D]).then_inc(w_hi_done, 1)
                if k == 1:
                    for n in range(0, KB, 2):
                        act.dma_start(xt[:, 0, n:n + 2, :], x[:, 0, n:n + 2, :]).then_inc(x_in[0], 16)
            act.wait_ge(x_in[0], 32)
            for k in range(KB):
                hi(x_hi[:, 0, k, :], xt[:, 0, k, :]).then_inc(x_hi_done, 1)
            act.wait_ge(ab_in, 16 * NB)
            hi(bs_hi[:].rearrange("p k b r -> p b k r"), ab[:, :, 1]).then_inc(ab_hi_done, 1)
            hi(as_hl[:, :, :, 0, :], ab[:, :, 0]).then_inc(ab_hi_done, 1)
            for i in range(KB):
                act.wait_ge(m_done, i + 1)
                hi(m_hi[:, i, 0:WH], ps[:, 2 * i, 0:WH]).then_inc(m_hi_done, 1)
                hi(m_hi[:, i, WH:D], ps[:, 2 * i + 1, 0:D - WH]).then_inc(m_hi_done, 1)
                hi(rt[:, :, i, 0, 0:TC],
                   ps[:, 2 * i + 1:2 * i + 2, D - WH:WH].to_broadcast([P, 2, TC])).then_inc(m_hi_done, 1)
                if i == 0:
                    act.wait_ge(bsum_done, KB)
                    hi(bsum_hl[:, 0], bsum[:]).then_inc(bsum_hi_done, 1)
            act.wait_ge(bt_in, 16)
            hi(bt_hi[:], btt[:]).then_inc(bt_hi_done, 1)
            act.wait_ge(x_in[1], 32)
            for k in range(KB):
                hi(x_hi[:, 1, k, :], xt[:, 1, k, :]).then_inc(x_hi_done, 1)
            act.wait_ge(g_done, 1)
            for s in range(2):
                hi(g_hl[:, 0, s * WH:(s + 1) * WH], ps[:, G_BANK + s, 0:WH]).then_inc(g_hi_done, 1)
            act.wait_ge(c_done, 1)
            for s in range(2):
                hi(bsum_hl[0:1, 0, s * WH:(s + 1) * WH], ps[0:1, C_BANK + s, 0:WH]).then_inc(c_hi_done, 1)

            def take_part(p):
                act.wait_ge(t_done, 2 * (p + 1))
                nc.scalar.activation(part[:, p], t_banks(p)[:, :, TA:2 * TA], ACT.Copy).then_inc(part_done, 1)

            def stack_t(p):
                act.wait_ge(ht_ps, p + 1)
                nc.scalar.activation(h_t[0:GK, p], t_banks(p)[0:GK, :, 2 * TA:2 * TA + P], ACT.Copy,
                                     scale=SCALING).then_inc(ht_done, 1)

            def exps(p):
                act.wait_ge(diff_done, p + 1)
                nc.scalar.activation(expd[:, p], diff[:, p], ACT.Exp).then_inc(exp_done, 1)

            def weighted_hi(p):
                act.wait_ge(hwt_ps, p + 1)
                hi(hw_hi[:, p // 2, (p % 2) * 2 * P:(p % 2 + 1) * 2 * P].rearrange("e (t n) -> e t n", t=2),
                   t_banks(p)[:, :, 2 * TA:2 * TA + P]).then_inc(hw_hi_done, 1)

            take_part(0)
            take_part(1)
            stack_t(0)
            stack_t(1)
            exps(0)
            exps(1)
            weighted_hi(0)
            weighted_hi(1)
            take_part(2)
            take_part(3)
            stack_t(2)
            stack_t(3)
            exps(2)
            exps(3)
            weighted_hi(2)
            weighted_hi(3)

        @block.vector
        def _(dve):
            steps = [0]

            def link(ins):
                steps[0] += 1
                ins.then_inc(dve_step, 1)
                dve.wait_ge(dve_step, steps[0])

            def lo(dst, src, high):
                return nc.vector.tensor_tensor(dst, src, high.bitcast(F32), ALU.subtract)

            nc.vector.memset(idle[:], 0.0).then_inc(idle_zero, 1)
            for n, c in enumerate((slice(D // 2, D), slice(0, D // 2))):
                dve.wait_ge(w0_in[n], 16)
                nc.vector.tensor_copy(wt_hi[:, 0, c], wt[:, 0, c]).then_inc(w0_hi_done, 1)
            for k in range(KB):
                if k == 0:
                    for s in range(2):
                        dve.wait_ge(wc_hi_done, s + 1)
                        c = slice(D + s * WH, D + (s + 1) * WH)
                        lo(wt_lo[:, 0, c], wt[:, 0, c], wt_hi[:, 0, c]).then_inc(wc_lo_done, 1)
                else:
                    dve.wait_ge(wc_hi_done, k + 2)
                    lo(wt_lo[:, k, D:CH], wt[:, k, D:CH], wt_hi[:, k, D:CH]).then_inc(wc_lo_done, 1)
                if k == 0:
                    dve.wait_ge(w0_hi_done, 2)
                else:
                    dve.wait_ge(w_hi_done, k)
                lo(wt_lo[:, k, 0:D], wt[:, k, 0:D], wt_hi[:, k, 0:D]).then_inc(w_lo_done, 1)
                if k == 0:
                    dve.wait_ge(const, 1)
                    nc.vector.tensor_copy(ones_r[:], ones[:]).then_inc(ones_rounded, 1)
            dve.wait_ge(bias_in, 16)
            dve.wait_ge(bbase_in, 16)
            for k in range(KB):
                if k > 0:
                    dve.wait_ge(bsum_done, k)
                nc.vector.scalar_tensor_tensor(out=bsum[:], in0=wt[:, k, D:CH], scalar=bcol[:, k:k + 1],
                                               in1=bsum[:], op0=ALU.mult, op1=ALU.add).then_inc(bsum_done, 1)
            dve.wait_ge(ab_hi_done, 1)
            lo(bs_lo[:].rearrange("p k b r -> p b k r"), ab[:, :, 1],
               bs_hi[:].rearrange("p k b r -> p b k r")).then_inc(ab_lo_done, 1)
            for i in range(KB):
                dve.wait_ge(m_hi_done, 3 * i + 1)
                lo(m_lo[:, i, 0:WH], ps[:, 2 * i, 0:WH], m_hi[:, i, 0:WH]).then_inc(m_lo_done, 1)
                dve.wait_ge(m_hi_done, 3 * i + 3)
                lo(m_lo[:, i, WH:D], ps[:, 2 * i + 1, 0:D - WH], m_hi[:, i, WH:D]).then_inc(m_lo_done, 1)
                lo(rt[:, :, i, 1, 0:TC], ps[:, 2 * i + 1:2 * i + 2, D - WH:WH].to_broadcast([P, 2, TC]),
                   rt[:, :, i, 0, 0:TC]).then_inc(m_lo_done, 1)
                if i == 0:
                    dve.wait_ge(ab_hi_done, 2)
                    lo(as_hl[:, :, :, 1, :], ab[:, :, 0], as_hl[:, :, :, 0, :]).then_inc(ab_lo_done, 1)
                    dve.wait_ge(bsum_hi_done, 1)
                    lo(bsum_hl[:, 1], bsum[:], bsum_hl[:, 0]).then_inc(bsum_lo_done, 1)
            dve.wait_ge(bt_hi_done, 1)
            lo(bt_lo[:], btt[:], bt_hi[:]).then_inc(bt_lo_done, 1)
            for s in range(2):
                dve.wait_ge(g_hi_done, s + 1)
                c = slice(s * WH, (s + 1) * WH)
                lo(g_hl[:, 1, c], ps[:, G_BANK + s, 0:WH], g_hl[:, 0, c]).then_inc(g_lo_done, 1)
            for s in range(2):
                dve.wait_ge(c_hi_done, s + 1)
                c = slice(s * WH, (s + 1) * WH)
                lo(bsum_hl[0:1, 1, c], ps[0:1, C_BANK + s, 0:WH], bsum_hl[0:1, 0, c]).then_inc(c_lo_done, 1)

            def stack(p):
                hs = h_stack[:, p].rearrange("p (t c) -> p t c", t=2)
                dve.wait_ge(part_done, p + 1)
                link(nc.vector.tensor_tensor(h_sum[:, p], t_banks(p)[:, :, TC:TA], part[:, p, :, TC:TA], ALU.add))
                if p == 0:
                    dve.wait_ge(const, 5)
                for at in (0, LROW):
                    last = nc.vector.tensor_copy(hs[:, :, at:at + R].bitcast(F32R), h_sum[:, p])
                    if at == 0:
                        link(last)
                nc.vector.tensor_tensor(hs[:, :, HROW:HROW + R].bitcast(F32R), h_sum[:, p],
                                        hs[:, :, 0:R], ALU.subtract).then_inc(stack_done, 1)

            def route(p):
                dve.wait_ge(slot_done, p + 1)
                link(nc.vector.tensor_tensor(full[:, p], t_banks(p)[:, :, 0:TC], part[:, p, :, 0:TC], ALU.add))
                for t in range(2):
                    link(nc.vector.max(top[:, p, t, :], full[:, p, t, 0:NE]))
                nc.vector.tensor_tensor(diff[:, p], top[:, p, :, 1], top[:, p, :, 0],
                                        ALU.subtract).then_inc(diff_done, 1)
                for t in range(2):
                    link(nc.vector.max_index(top_at[:, p, t, :], top[:, p, t, :], full[:, p, t, 0:NE]))
                for t in range(2):
                    link(nc.vector.tensor_tensor(
                        onehot[:, p, t], iota[:, None, :].to_broadcast([P, 2, NE]),
                        top_at[:, p, t, 0:2, None].to_broadcast([P, 2, NE]), ALU.is_equal))
                dve.wait_ge(exp_done, p + 1)
                link(nc.vector.tensor_scalar(den[:, p], expd[:, p], 1.0 / SCALING, 1.0 / SCALING,
                                             ALU.mult, ALU.add))
                link(nc.vector.reciprocal(wk[:, p, :, 0], den[:, p]))
                link(nc.vector.tensor_tensor(wk[:, p, :, 1], wk[:, p, :, 0], expd[:, p], ALU.mult))
                link(nc.vector.tensor_tensor(whot[:, p], onehot[:, p],
                                             wk[:, p, :, :, None].to_broadcast([P, 2, 2, NE]), ALU.mult))
                link(nc.vector.tensor_tensor(we[:, p], whot[:, p, :, 0, :], whot[:, p, :, 1, :], ALU.add))
                nc.vector.tensor_tensor(
                    hw[:, p].rearrange("p t (e r) -> p t e r", e=NE),
                    full[:, p, :, NE:TC].rearrange("p t (e r) -> p t e r", e=NE),
                    we[:, p, :, :, None].to_broadcast([P, 2, NE, R]), ALU.mult).then_inc(hw_done, 1)

            def weighted_lo(p):
                c = slice((p % 2) * 2 * P, (p % 2 + 1) * 2 * P)
                dve.wait_ge(hw_hi_done, p + 1)
                lo(hw_lo[:, p // 2, c].rearrange("e (t n) -> e t n", t=2), t_banks(p)[:, :, 2 * TA:2 * TA + P],
                   hw_hi[:, p // 2, c].rearrange("e (t n) -> e t n", t=2)).then_inc(hw_lo_done, 1)

            def finish(n):
                j, tok = PIECES[n]
                h, o = divmod(j, OB)
                dve.wait_ge(f_done, n + 1)
                nc.vector.tensor_tensor(xt[:, h, o, tok], piece_ps(n), xt[:, h, o, tok],
                                        ALU.add).then_inc(out_ready, 1)

            stack(0)
            stack(1)
            route(0)
            route(1)
            weighted_lo(0)
            weighted_lo(1)
            stack(2)
            stack(3)
            finish(0)
            route(2)
            finish(1)
            finish(2)
            route(3)
            finish(3)
            weighted_lo(2)
            weighted_lo(3)
            for n in range(OB, len(PIECES)):
                finish(n)

        @block.tensor
        def _(pe):
            mm = nc.tensor.matmul
            pe.wait_ge(idle_zero, 1)
            for _ in range(IDLE):
                mm(ps[:, 7, 0:P], idle[:], idle[:], start=True, stop=True)

            def m_part(k, i, s, a, c, first=False, last=False):
                return mm(ps[:, 2 * i + s, 0:WH], a[:, k, i * P:(i + 1) * P],
                          c[:, k, D + s * WH:D + (s + 1) * WH], start=first, stop=last)

            for k in range(KB - 1):
                if k > 0:
                    pe.wait_ge(w_hi_done, k)
                for s in range(2):
                    pe.wait_ge(wc_hi_done, s + 1 if k == 0 else k + 2)
                    for n, i in enumerate((2, 3, 0, 1)):
                        if k == 0 and s == 0:
                            pe.wait_ge(w0_hi_done, 1 + n // 2)
                        m_part(k, i, s, wt_hi, wt_hi, first=(k == 0))
                pe.wait_ge(wc_lo_done, k + 2)
                for s in range(2):
                    for i in range(KB):
                        m_part(k, i, s, wt_hi, wt_lo)
                pe.wait_ge(w_lo_done, k + 1)
                for s in range(2):
                    for i in range(KB):
                        m_part(k, i, s, wt_lo, wt_hi)
            k = KB - 1
            pe.wait_ge(w_hi_done, KB - 1)
            pe.wait_ge(wc_hi_done, KB + 1)
            pe.wait_ge(wc_lo_done, KB + 1)
            pe.wait_ge(w_lo_done, KB)
            for i in range(KB):
                for s in range(2):
                    m_part(k, i, s, wt_hi, wt_hi)
                    m_part(k, i, s, wt_hi, wt_lo)
                    last = m_part(k, i, s, wt_lo, wt_hi, last=True)
                last.then_inc(m_done, 1)
            pe.wait_ge(ab_hi_done, 1)
            pe.wait_ge(ab_lo_done, 1)
            pe.wait_ge(m_lo_done, 3)
            for s in range(2):
                for k in range(KB):
                    for n, (a, c) in enumerate(((bs_hi, wt_hi), (bs_hi, wt_lo), (bs_lo, wt_hi))):
                        last = mm(ps[:, G_BANK + s, 0:WH], a[:, k].rearrange("p b r -> p (b r)"),
                                  c[:, k, D + s * WH:D + (s + 1) * WH],
                                  start=(k == 0 and n == 0), stop=(k == KB - 1 and n == 2))
            last.then_inc(g_done, 1)
            pe.wait_ge(ones_rounded, 1)
            pe.wait_ge(bsum_hi_done, 1)
            pe.wait_ge(bsum_lo_done, 1)
            pe.wait_ge(m_lo_done, 6)
            for s in range(2):
                for i in range(2):
                    last = mm(ps[:, C_BANK + s, 0:WH], ones_r[:], bsum_hl[:, i, s * WH:(s + 1) * WH],
                              start=(i == 0), stop=(i == 1))
            last.then_inc(c_done, 1)

            def router(p):
                if p == 0:
                    pe.wait_ge(m_lo_done, 3 * KB)
                    pe.wait_ge(x_hi_done, KB)
                    pe.wait_ge(x_lo_done, KB)
                if p >= 2:
                    pe.wait_ge(hw_lo_done, p - 1)
                    pe.wait_ge(x_hi_done, 2 * KB)
                    pe.wait_ge(x_lo_done, 2 * KB)
                for t in range(2):
                    b = 2 * p + t
                    pe.wait_ge(as_put, b + 1)
                    h, tok = b // (NB // 2), slice((b % 4) * P, (b % 4 + 1) * P)
                    for i in range(KB):
                        op = rt[:, b % 2, i].rearrange("p l c -> p (l c)")
                        mm(t_banks(p)[:, t, 0:2 * TA], x_hi[:, h, i, tok], op, start=(i == 0), stop=False,
                           skip_group_check=True)
                        last = mm(t_banks(p)[:, t, 0:TA], x_lo[:, h, i, tok], op[:, 0:TA], start=False,
                                  stop=False, skip_group_check=True)
                    last.then_inc(t_done, 1)

            def stack_transpose(p):
                if p == 0:
                    pe.wait_ge(const, 2)
                pe.wait_ge(stack_done, p + 1)
                for t in range(2):
                    last = mm(t_banks(p)[:, t, 2 * TA:2 * TA + P], h_stack[:, p, t * P:(t + 1) * P], ident[:],
                              is_transpose=True, start=False, stop=True, skip_group_check=True)
                last.then_inc(ht_ps, 1)

            def slots(p):
                if p == 0:
                    pe.wait_ge(cst_in, 32)
                pe.wait_ge(ht_done, p + 1)
                pe.wait_ge(gst_in[p], 48)
                for t in range(2):
                    last = mm(t_banks(p)[:, t, 0:TC], h_t[0:GK, p, t, :], g_st[0:GK, p, D:WC],
                              start=False, stop=True, skip_group_check=True)
                last.then_inc(slot_done, 1)

            def weighted_transpose(p):
                pe.wait_ge(hw_done, p + 1)
                for t in range(2):
                    last = nc.tensor.transpose(t_banks(p)[:, t, 2 * TA:2 * TA + P], hw[:, p, t, :], ident[:])
                last.then_inc(hwt_ps, 1)

            def base(n, part_of):
                j, tok = PIECES[n]
                h, o = divmod(j, OB)
                if n == 0:
                    pe.wait_ge(g_lo_done, 2)
                if n == 2:
                    pe.wait_ge(c_lo_done, 2)
                if OB <= n < NB and part_of == 0:
                    pe.wait_ge(out_ready, n - OB + 1)
                if n == NB:
                    pe.wait_ge(hw_lo_done, 3)
                products = [(a, v, i) for a, v in ((m_hi, x_hi), (m_lo, x_hi), (m_hi, x_lo)) for i in range(KB)]
                for m in range(6 * part_of, 6 * part_of + 6):
                    a, v, i = products[m]
                    mm(piece_ps(n), a[:, i, o * P:(o + 1) * P], v[:, h, i, tok], start=(m == 0), stop=False)

            def rest(n):
                j, tok = PIECES[n]
                h, o = divmod(j, OB)
                oc = slice(o * P, (o + 1) * P)
                for at in range(tok.start, tok.stop, 2 * P):
                    p = 2 * h + at // (2 * P)
                    mm(piece_ps(n)[:, at - tok.start:at - tok.start + 2 * P], g_st[0:GK, p, oc],
                       h_t[0:GK, p].rearrange("k t n -> k (t n)"), start=False, stop=False)
                if n == 0:
                    pe.wait_ge(bt_hi_done, 1)
                    pe.wait_ge(bt_lo_done, 1)
                pe.wait_ge(hw_lo_done, 2 * (h + 1))
                mm(piece_ps(n), bt_hi[:, oc], hw_hi[:, h, tok], start=False, stop=False)
                mm(piece_ps(n), bt_lo[:, oc], hw_hi[:, h, tok], start=False, stop=False)
                mm(piece_ps(n), bt_hi[:, oc], hw_lo[:, h, tok], start=False, stop=True).then_inc(f_done, 1)

            router(0)
            router(1)
            base(0, 0)
            stack_transpose(0)
            base(0, 1)
            slots(0)
            stack_transpose(1)
            base(1, 0)
            slots(1)
            base(1, 1)
            base(2, 0)
            weighted_transpose(0)
            base(2, 1)
            base(3, 0)
            weighted_transpose(1)
            base(3, 1)
            router(2)
            router(3)
            rest(0)
            stack_transpose(2)
            rest(1)
            stack_transpose(3)
            slots(2)
            rest(2)
            slots(3)
            rest(3)
            base(4, 0)
            base(4, 1)
            weighted_transpose(2)
            base(5, 0)
            base(5, 1)
            base(6, 0)
            weighted_transpose(3)
            base(6, 1)
            rest(4)
            base(7, 0)
            base(7, 1)
            rest(5)
            rest(6)
            base(8, 0)
            rest(7)
            base(8, 1)
            rest(8)


def kernel(**inputs):
    import numpy as np
    import concourse.bacc as bacc
    from concourse.bass_utils import run_bass_kernel_spmd

    def a(name):
        return np.asarray(inputs[name])

    def blocks(m):
        return m.reshape(m.shape[0] // P, P, m.shape[1]).transpose(1, 0, 2)

    x = a("x").reshape(HALVES, HT, KB, P).transpose(3, 0, 2, 1)
    wc = np.concatenate([a("L0_ffn_W_base"), a("L0_ffn_W_router"), a("L0_ffn_A").reshape(NE * R, D)])
    w = np.concatenate([blocks(a("L0_cond_W")), blocks(wc.T)], axis=2)
    by_slot = [m.reshape(SLOTS, KB, P, R).transpose(0, 2, 1, 3).reshape(SLOTS, P, KB * R)
               for m in (a("L0_cond_lora_As"), a("L0_cond_lora_Bs").transpose(0, 2, 1))]
    arrays = {
        "x_t": x,
        "w_chunks": w,
        "adapters": np.concatenate(by_slot, axis=2),
        "slots": a("itok_B_0_23").reshape(1, NB),
        "bias": a("L0_cond_b").reshape(KB, P).T,
        "b_base": a("L0_ffn_b_base").reshape(1, D),
        "b_t": a("L0_ffn_B").transpose(0, 2, 1).reshape(NE * R, D),
    }
    arrays = {k: np.ascontiguousarray(v) for k, v in arrays.items()}
    nc = bacc.Bacc("TRN2", target_bir_lowering=False, num_devices=1)
    args = [nc.dram_tensor(k, v.shape, mybir.dt.from_np(v.dtype), kind="ExternalInput").ap()
            for k, v in arrays.items()]
    args.append(nc.dram_tensor("out_t", (NB, P, HT), F32, kind="ExternalOutput").ap())
    build(nc, *args)
    got = run_bass_kernel_spmd(nc, [arrays], core_ids=[0]).results[0]["out_t"]
    return np.asarray(got).reshape(HALVES, OB, P, HT).transpose(0, 3, 1, 2).reshape(NB, P, D)
```
